# Optimizing a Trainium2 kernel written in Bass

```python
import numpy as np
import jax
import jax.numpy as jnp

def _softmax(x, axis=-1):
    return jax.nn.softmax(x, axis=axis)

def _gelu(x):
    return jax.nn.gelu(x, approximate=True)

def _silu(x):
    return jax.nn.silu(x)

def _sigmoid(x):
    return jax.nn.sigmoid(x)

def _layernorm(x, axis=-1, eps=1e-05):
    m = jnp.mean(x, axis=axis, keepdims=True)
    v = jnp.var(x, axis=axis, keepdims=True)
    return (x - m) / jnp.sqrt(v + eps)

def _scatter_add(tgt, idx, src, axis=0):
    return tgt.at[idx].add(src)

def _segment_sum(src, seg, n):
    return jax.ops.segment_sum(src, seg, n)
kernel_name = 'mk_flamingo_gated_d1_seqx_r8_09de60'

def setup_inputs(seed: int=0):
    np.random.seed(seed)
    _w = jnp.asarray

    def _rec_inputs():
        import jax
        import jax.numpy as jnp
        _rk = jax.random.key(seed)
        x = -0.000125 + 0.9999 * jax.random.normal(jax.random.fold_in(_rk, 1), (8, 256, 256), jnp.float32)
        _lenS = 256 - jax.random.randint(jax.random.fold_in(_rk, 7), (8,), 0, max(1, 256 // 4) + 1, jnp.int32)
        _lenS2 = 64 - jax.random.randint(jax.random.fold_in(_rk, 8), (8,), 0, max(1, 64 // 4) + 1, jnp.int32)
        _ctx_2048P = jax.random.normal(jax.random.fold_in(_rk, 11), (8, 16, 256), jnp.float32)
        _ctx_2048c = jax.random.dirichlet(jax.random.fold_in(_rk, 511), 0.3 * jnp.ones((16,), jnp.float32), (8, 64))
        _ctx_2048t = jnp.einsum('bsk,bkd->bsd', _ctx_2048c, _ctx_2048P)
        _ctx_2048t = _ctx_2048t * jax.lax.rsqrt(jnp.mean(jnp.square(_ctx_2048t)) + 1e-12) * 0.953939
        ctx_2048 = 0.00222621 + 0.99962 * (_ctx_2048t + 0.3 * jax.random.normal(jax.random.fold_in(_rk, 611), (8, 64, 256), jnp.float32))
        itok_Sx4_0_63 = jax.random.randint(jax.random.fold_in(_rk, 12), (256, 4), 0, 64, jnp.int32)
        _g = jax.random.normal(jax.random.fold_in(_rk, 9001), (2, 1), jnp.float32)
        _g = jnp.sign(_g) * jnp.maximum(jnp.abs(_g), 1.0) + (_g == 0) * 1.0
        g_xattn = _g[0]
        g_ffn = _g[1]
        return (x, ctx_2048, itok_Sx4_0_63, g_xattn, g_ffn)
    x, ctx_2048, itok_Sx4_0_63, g_xattn, g_ffn = _rec_inputs()

    def _L0_xattn_setup():
        import math
        import jax, jax.numpy as jnp
        import numpy as np
        B, S, D, N, K, TOPK = (4, 512, 256, 64, 4, 2)
        key = jax.random.key(seed)
        k0, k1, k2, k3, k4 = jax.random.split(key, 5)
        token_states = jax.random.normal(k0, (B, S, D), dtype=jnp.float32)
        set_states = jax.random.normal(k1, (B, N, D), dtype=jnp.float32)
        desc_router = jax.random.normal(k2, (N, D), dtype=jnp.float32)
        token_to_sets = jax.random.randint(k3, (S, K), 0, N)
        bound = 1.0 / math.sqrt(D)
        W_q = jax.random.uniform(k4, (D, D), jnp.float32, -bound, bound)
        b_q = jnp.zeros((D,), jnp.float32)
        return {'token_states': token_states, 'set_states': set_states, 'desc_router': desc_router, 'W_q': W_q, 'b_q': b_q, 'token_to_sets': token_to_sets}
    _L0_xattn_all = _L0_xattn_setup()
    _L0_xattn_in = {k: v for k, v in _L0_xattn_all.items() if k in ('desc_router', 'W_q', 'b_q')}
    del _L0_xattn_all

    def _L0_ffn_setup():
        import jax, jax.numpy as jnp
        import numpy as np
        BLOCK_SIZE = 32
        HIDDEN_SIZE = 256
        MLP_DIM = 2048
        NVFP4_LUT = jnp.array([0.0, 0.5, 1.0, 1.5, 2.0, 3.0, 4.0, 6.0, 0.0, -0.5, -1.0, -1.5, -2.0, -3.0, -4.0, -6.0], dtype=jnp.float32)

        def dequant_nvfp4(W_packed, scales, block=BLOCK_SIZE):
            N = W_packed.shape[0]
            low = W_packed & 15
            high = W_packed >> 4 & 15
            idx = jnp.stack([low, high], axis=-1).reshape(N, -1)
            vals = NVFP4_LUT[idx]
            K = vals.shape[1]
            vals = vals.reshape(N, K // block, block) * scales[:, :, None]
            return vals.reshape(N, K)
        key = jax.random.key(seed)
        ks = jax.random.split(key, 7)
        x = jax.random.normal(ks[0], (4, 32, HIDDEN_SIZE), dtype=jnp.float32)
        gate_W_packed = jax.random.randint(ks[1], (MLP_DIM, HIDDEN_SIZE // 2), 0, 32, dtype=jnp.int32)
        gate_scales = jax.random.uniform(ks[2], (MLP_DIM, HIDDEN_SIZE // BLOCK_SIZE), dtype=jnp.float32) * 0.1 + 0.001
        up_W_packed = jax.random.randint(ks[3], (MLP_DIM, HIDDEN_SIZE // 2), 0, 32, dtype=jnp.int32)
        up_scales = jax.random.uniform(ks[4], (MLP_DIM, HIDDEN_SIZE // BLOCK_SIZE), dtype=jnp.float32) * 0.1 + 0.001
        down_W_packed = jax.random.randint(ks[5], (HIDDEN_SIZE, MLP_DIM // 2), 0, 32, dtype=jnp.int32)
        down_scales = jax.random.uniform(ks[6], (HIDDEN_SIZE, MLP_DIM // BLOCK_SIZE), dtype=jnp.float32) * 0.1 + 0.001
        return {'x': x, 'gate_W_packed': gate_W_packed, 'gate_scales': gate_scales, 'up_W_packed': up_W_packed, 'up_scales': up_scales, 'down_W_packed': down_W_packed, 'down_scales': down_scales}
    _L0_ffn_all = _L0_ffn_setup()
    _L0_ffn_in = {k: v for k, v in _L0_ffn_all.items() if k in ('gate_W_packed', 'gate_scales', 'up_W_packed', 'up_scales', 'down_W_packed', 'down_scales')}
    del _L0_ffn_all
    return {'x': x, 'ctx_2048': ctx_2048, 'itok_Sx4_0_63': itok_Sx4_0_63, 'g_xattn': g_xattn, 'g_ffn': g_ffn, 'L0_xattn_desc_router': _L0_xattn_in['desc_router'], 'L0_xattn_W_q': _L0_xattn_in['W_q'], 'L0_xattn_b_q': _L0_xattn_in['b_q'], 'L0_ffn_gate_W_packed': _L0_ffn_in['gate_W_packed'], 'L0_ffn_gate_scales': _L0_ffn_in['gate_scales'], 'L0_ffn_up_W_packed': _L0_ffn_in['up_W_packed'], 'L0_ffn_up_scales': _L0_ffn_in['up_scales'], 'L0_ffn_down_W_packed': _L0_ffn_in['down_W_packed'], 'L0_ffn_down_scales': _L0_ffn_in['down_scales']}

def reference(x, ctx_2048, itok_Sx4_0_63, g_xattn, g_ffn, L0_xattn_desc_router, L0_xattn_W_q, L0_xattn_b_q, L0_ffn_gate_W_packed, L0_ffn_gate_scales, L0_ffn_up_W_packed, L0_ffn_up_scales, L0_ffn_down_W_packed, L0_ffn_down_scales):
    import jax
    import jax.numpy as jnp

    def _L0_xattn_ref(token_states, set_states, desc_router, W_q, b_q, token_to_sets):
        import math
        import jax, jax.numpy as jnp
        import numpy as np
        B, S, D, N, K, TOPK = (4, 512, 256, 64, 4, 2)
        batch, seq_len, d = token_states.shape
        num_sets = set_states.shape[1]
        scale = 1.0 / math.sqrt(d)
        q = jnp.einsum('bsd,ed->bse', token_states, W_q) + b_q
        scores = jnp.einsum('bse,ne->bsn', q, desc_router) * scale
        valid = token_to_sets >= 0
        mask = ((token_to_sets[:, :, None] == jnp.arange(num_sets)[None, None, :]) & valid[:, :, None]).any(axis=1)
        neg_inf = jnp.array(-jnp.inf, scores.dtype)
        scores = jnp.where(mask[None, :, :], scores, neg_inf)
        topk_vals, topk_idx = jax.lax.top_k(scores, TOPK)
        b_i = jnp.arange(batch)[:, None, None]
        s_i = jnp.arange(seq_len)[None, :, None]
        scores = jnp.full_like(scores, neg_inf).at[b_i, s_i, topk_idx].set(topk_vals)
        weights = jax.nn.softmax(scores, axis=-1)
        return jnp.einsum('bsn,bnd->bsd', weights, set_states)

    def _L0_ffn_ref(x, gate_W_packed, gate_scales, up_W_packed, up_scales, down_W_packed, down_scales):
        import jax, jax.numpy as jnp
        import numpy as np
        BLOCK_SIZE = 32
        HIDDEN_SIZE = 256
        MLP_DIM = 2048
        NVFP4_LUT = jnp.array([0.0, 0.5, 1.0, 1.5, 2.0, 3.0, 4.0, 6.0, 0.0, -0.5, -1.0, -1.5, -2.0, -3.0, -4.0, -6.0], dtype=jnp.float32)

        def dequant_nvfp4(W_packed, scales, block=BLOCK_SIZE):
            N = W_packed.shape[0]
            low = W_packed & 15
            high = W_packed >> 4 & 15
            idx = jnp.stack([low, high], axis=-1).reshape(N, -1)
            vals = NVFP4_LUT[idx]
            K = vals.shape[1]
            vals = vals.reshape(N, K // block, block) * scales[:, :, None]
            return vals.reshape(N, K)
        B, S, H = x.shape
        xt = x.reshape(B * S, H)
        Wg = dequant_nvfp4(gate_W_packed, gate_scales)
        Wu = dequant_nvfp4(up_W_packed, up_scales)
        Wd = dequant_nvfp4(down_W_packed, down_scales)
        gate = jnp.einsum('th,nh->tn', xt, Wg)
        up = jnp.einsum('th,nh->tn', xt, Wu)
        gelu = jnp.tanh(0.7978845608028654 * (gate + 0.044715 * gate ** 3)) * gate * 0.5 + gate * 0.5
        inter = gelu * up
        out = jnp.einsum('tn,hn->th', inter, Wd)
        return out.reshape(B, S, H)
    x = x + jnp.tanh(g_xattn[0]) * _L0_xattn_ref(_layernorm(x, axis=-1), ctx_2048, L0_xattn_desc_router, L0_xattn_W_q, L0_xattn_b_q, itok_Sx4_0_63)
    x = x + jnp.tanh(g_ffn[0]) * _L0_ffn_ref(_layernorm(x, axis=-1), L0_ffn_gate_W_packed, L0_ffn_gate_scales, L0_ffn_up_W_packed, L0_ffn_up_scales, L0_ffn_down_W_packed, L0_ffn_down_scales)
    return x

_drawn_inputs = setup_inputs


def setup_inputs(seed=0):
    import zlib

    import numpy as np

    out = dict(_drawn_inputs(seed))
    spreads = {'L0_xattn_b_q': (0.0, 0.1)}
    factors = {}
    for name, (base, spread) in spreads.items():
        noise = np.random.default_rng([zlib.crc32(name.encode()), seed]).standard_normal(out[name].shape)
        drawn = base * np.exp(spread * noise) if base else spread * noise
        out[name] = jnp.asarray(drawn.astype(out[name].dtype))
    for name, factor in factors.items():
        out[name] = (out[name] * factor).astype(out[name].dtype)
    return out
```

```python
from contextlib import ExitStack

import concourse.bass as bass
from concourse import mybir

ALU = mybir.AluOpType
ACT = mybir.ActivationFunctionType
F32 = mybir.dt.float32
F32R = mybir.dt.float32r
F16 = mybir.dt.float16
I32 = mybir.dt.int32
U32 = mybir.dt.uint32

P = 128
LN_EPS = 1e-5
MASKED = -3.0e38
GELU_CUBIC = 0.044715
GELU_SCALE = 0.7978845608028654
FP4_MASK = 0x8E008E00 - (1 << 32)
FP4_SHIFT = 16384.0


def build_program(
    nc: bass.Bass,
    x: bass.AP,
    ctx_sets: bass.AP,
    token_sets: bass.AP,
    g_xattn: bass.AP,
    g_ffn: bass.AP,
    router: bass.AP,
    w_q: bass.AP,
    b_q: bass.AP,
    gate_packed: bass.AP,
    gate_scales: bass.AP,
    up_packed: bass.AP,
    up_scales: bass.AP,
    down_packed: bass.AP,
    down_scales: bass.AP,
    out: bass.AP,
):
    BATCH, SEQ, D = x.shape
    SETS = ctx_sets.shape[1]
    PICKS = token_sets.shape[1]
    MLP = gate_packed.shape[0]
    KT = D // P
    TILES = BATCH * SEQ // P
    CT = 4
    CHUNKS = TILES // CT
    TOK = CT * P
    HALVES = SEQ // P
    CB = CT // HALVES
    UNITS = MLP // P
    CODES = 3 * D // 2
    WU = 3 * D
    BLK = 32
    SU = WU // BLK
    PG = 2
    PRING = 4
    RING = 4
    SCORE_SCALE = float(D) ** -0.5
    assert KT == 2 and HALVES == 2 and UNITS % RING == 0 and down_packed.shape[0] == D

    AT_STATS, AT_NORM = 1, 3
    AT_OUT = 3
    AT_LN1, AT_SCORES, AT_WEIGHTS, AT_PT, AT_PV = 4, 6, 7, 9, 10
    AT_NORM2, AT_LN2 = 12, 13
    LEAD = 2
    DECODE_LEAD = 3

    x_v = x.rearrange("b (h p) d -> p (b h) d", p=P)
    out_v = out.rearrange("b (h p) d -> p (b h) d", p=P)
    ctx_v = ctx_sets.rearrange("b n d -> n b d")

    with ExitStack() as stack:
        def sb(name, shape, dt=F32):
            return stack.enter_context(nc.sbuf_tensor(name, shape, dt))

        def psum(name, shape):
            return stack.enter_context(nc.psum_tensor(name, shape, F32))

        def sem(name):
            return stack.enter_context(nc.semaphore(name))

        x_sb = sb("x_sb", [P, TILES, D])
        ctx_sb = sb("ctx_sb", [SETS, BATCH, D])
        tok_sb = sb("tok_sb", [P, HALVES, PICKS], I32)
        tok_f = sb("tok_f", [P, HALVES, PICKS])
        router_sb = sb("router_sb", [SETS, D])
        wq_sb = sb("wq_sb", [P, KT, D])
        bq_sb = sb("bq_sb", [P, KT])
        bq_wide = sb("bq_wide", [P, KT, P])
        router_t = sb("router_t", [P, KT, SETS])
        score_w = sb("score_w", [P, KT, SETS])
        iota_i = sb("iota_i", [P, SETS], I32)
        iota_f = sb("iota_f", [P, SETS])
        allowed = sb("allowed", [P, HALVES, SETS])
        score_bias = sb("score_bias", [P, HALVES, SETS])
        gates_in = sb("gates_in", [P, 2])
        gates = sb("gates", [P, 2])
        ident = sb("ident", [P, P])
        minus_half = sb("minus_half", [P, CT])

        stats = sb("stats", [P, CT, 6])
        mean_var = sb("mean_var", [P, CT, 2])
        var_eps = sb("var_eps", [P, CT])
        rstd = sb("rstd", [P, CT])
        normed = sb("normed", [P, CT, D])
        turned = sb("turned", [P, KT, TOK])
        scores = sb("scores", [P, CT, SETS])
        top8 = sb("top8", [P, CT, 8])
        top8_at = sb("top8_at", [P, CT, 8], U32)
        top2_at = sb("top2_at", [P, CT, 2])
        gap = sb("gap", [P, CT])
        second = sb("second", [P, CT])
        total = sb("total", [P, CT])
        inv_total = sb("inv_total", [P, CT])
        w_first = sb("w_first", [P, CT])
        w_second = sb("w_second", [P, CT])
        probs_a = sb("probs_a", [P, CT, SETS])
        probs_b = sb("probs_b", [P, CT, SETS])
        probs = sb("probs", [P, CT, SETS])
        probs_t = sb("probs_t", [SETS, TOK])

        packed = sb("packed", [P, PRING, CODES], I32)
        scales_sb = sb("scales_sb", [P, UNITS, SU])
        high_codes = sb("high_codes", [P, CODES], I32)
        code_bits = sb("code_bits", [P, CODES], I32)
        w_nat = sb("w_nat", [P, 2, WU])
        w_hi = sb("w_hi", [P, UNITS, WU], F32R)
        w_lo = sb("w_lo", [P, UNITS, WU], F32R)
        xt_hi = sb("xt_hi", [P, CHUNKS, KT, TOK], F32R)
        xt_lo = sb("xt_lo", [P, CHUNKS, KT, TOK], F32R)
        act = sb("act", [P, 2, TOK])
        act_hi = sb("act_hi", [P, RING, TOK], F32R)
        act_lo = sb("act_lo", [P, 2, TOK], F32R)

        gate_ps = psum("gate_ps", [P, 2, TOK])
        up_ps = psum("up_ps", [P, 2, TOK])
        acc_ps = psum("acc_ps", [P, KT, TOK])
        misc_ps = psum("misc_ps", [P, 2, TOK])

        x_loaded = sem("x_loaded")
        x_rest_loaded = sem("x_rest_loaded")
        ctx_loaded = sem("ctx_loaded")
        router_loaded = sem("router_loaded")
        small_loaded = sem("small_loaded")
        wq_loaded = sem("wq_loaded")
        scales_loaded = sem("scales_loaded")
        packed_loaded = [sem(f"packed_loaded{g}") for g in range(UNITS // PG)]
        stored = sem("stored")

        ident_made = sem("ident_made")
        iota_made = sem("iota_made")
        minus_half_made = sem("minus_half_made")
        setup = sem("setup")
        bq_spread = sem("bq_spread")
        router_turned = sem("router_turned")
        router_copied = sem("router_copied")
        score_w_done = sem("score_w_done")
        score_w_copied = sem("score_w_copied")
        gates_ready = sem("gates_ready")

        lined_up = sem("lined_up")
        unpacked = sem("unpacked")
        scaled = sem("scaled")
        unit_turned = sem("unit_turned")
        hi_stored = sem("hi_stored")
        lo_stored = sem("lo_stored")

        attn = sem("attn")
        var_ready = sem("var_ready")
        rstd_ready = sem("rstd_ready")
        normed_ready = sem("normed_ready")
        ln1_turned = sem("ln1_turned")
        ln1_copied = sem("ln1_copied")
        scores_done = sem("scores_done")
        scores_read = sem("scores_read")
        gap_ready = sem("gap_ready")
        second_ready = sem("second_ready")
        probs_ready = sem("probs_ready")
        probs_turned = sem("probs_turned")
        probs_copied = sem("probs_copied")
        attended = sem("attended")
        x_updated = sem("x_updated")
        ln2_turned = sem("ln2_turned")
        xt_hi_ready = sem("xt_hi_ready")
        xt_lo_ready = sem("xt_lo_ready")

        gate_done = sem("gate_done")
        up_done = sem("up_done")
        squared = sem("squared")
        cubic_done = sem("cubic_done")
        tanh_done = sem("tanh_done")
        gelu_done = sem("gelu_done")
        inter_done = sem("inter_done")
        inter_hi = sem("inter_hi")
        inter_lo = sem("inter_lo")
        down_done = sem("down_done")
        acc_copied = sem("acc_copied")
        out_turned = sem("out_turned")
        out_ready = sem("out_ready")

        def turned_unit(u):
            return (gate_ps, up_ps, misc_ps)[min(u, LEAD)]

        block = stack.enter_context(nc.Block())

        @block.sync
        def _(sp):
            def load_x(c0, c1, done):
                t = slice(c0 * CT, c1 * CT)
                sp.dma_start(x_sb[:, t, :], x_v[:, t, :]).then_inc(done, 16)

            def load_packed(g):
                at = g * PG % PRING
                ring = slice(at, at + PG)
                units = slice(g * PG * P, (g + 1) * PG * P)
                if g * PG >= PRING:
                    sp.wait_ge(unpacked, (g + 1) * PG - PRING)
                for m, src in ((0, gate_packed), (1, up_packed)):
                    sp.dma_start(packed[:, ring, m * P:(m + 1) * P],
                                 src[units, :].rearrange("(u p) j -> p u j", p=P)).then_inc(packed_loaded[g], 16)
                half = P // 2
                for a in range(KT):
                    sp.dma_start(packed[:, ring, 2 * P + a * half:2 * P + (a + 1) * half],
                                 down_packed[a * P:(a + 1) * P, g * PG * half:(g + 1) * PG * half]
                                 .rearrange("p (u j) -> p u j", u=PG)).then_inc(packed_loaded[g], 16)

            load_x(0, 1, x_loaded)
            sp.dma_start(wq_sb[:, :, :], w_q.rearrange("(k p) d -> p k d", p=P)).then_inc(wq_loaded, 16)
            load_packed(0)
            sp.dma_start(ctx_sb[:, :, :], ctx_v).then_inc(ctx_loaded, 16)
            load_packed(1)
            load_x(1, CHUNKS, x_rest_loaded)
            for g in range(PRING // PG, UNITS // PG):
                load_packed(g)
            for b in range(2 * CHUNKS):
                sp.wait_ge(out_ready, b + 1)
                t = slice(b * HALVES, (b + 1) * HALVES)
                sp.dma_start(out_v[:, t, :], x_sb[:, t, :]).then_inc(stored, 16)
            sp.wait_ge(stored, 16 * 2 * CHUNKS)

        @block.gpsimd
        def _(pool):
            pool.memset(ident[:, :], 0.0).then_inc(ident_made, 1)
            pool.iota(iota_i[:, :], [[1, SETS]], base=0, channel_multiplier=0).then_inc(iota_made, 1)
            pool.wait_ge(ident_made, 1)
            pool.affine_select(out=ident[:, :], in_=ident[:, :], compare_op=ALU.not_equal, fill=1.0, base=0,
                               pattern=[[-1, P]], channel_multiplier=1).then_inc(ident_made, 1)
            pool.memset(minus_half[:, :], -0.5).then_inc(minus_half_made, 1)

            def scale_unit(u):
                if u == 0:
                    pool.wait_ge(scales_loaded, 16 * 4)
                pool.wait_ge(unpacked, u + 1)
                if u >= 2:
                    pool.wait_ge(unit_turned, u - 1)
                codes = code_bits[:, :].bitcast(F16).rearrange("p (b k) -> p b k", k=BLK)
                w = w_nat[:, u % 2, :].rearrange("p (b k) -> p b k", k=BLK)
                s = scales_sb[:, u, :].unsqueeze(2).to_broadcast([P, SU, BLK])
                pool.tensor_tensor(w, codes, s, ALU.mult).then_inc(scaled, 1)

            def root(n):
                pool.wait_ge(var_ready, n + 1)
                if n == 0:
                    pool.wait_ge(minus_half_made, 1)
                else:
                    pool.wait_ge(normed_ready, n)
                pool.tensor_tensor(rstd[:, :], var_eps[:, :], minus_half[:, :], ALU.pow).then_inc(rstd_ready, 1)

            def low_part(c, n):
                s = c * UNITS + n
                pool.wait_ge(inter_hi, s + 1)
                if c > 0 or n >= 2:
                    pool.wait_ge(down_done, s - 1)
                pool.tensor_tensor(act_lo[:, n % 2, :], act[:, n % 2, :],
                                   act_hi[:, n % RING, :].bitcast(F32), ALU.subtract).then_inc(inter_lo, 1)

            root(0)
            scale_unit(0)
            scale_unit(1)
            root(1)
            scale_unit(2)
            for c in range(CHUNKS):
                for n in range(UNITS):
                    if c == 0 and n + DECODE_LEAD < UNITS:
                        scale_unit(n + DECODE_LEAD)
                    if c + 1 < CHUNKS and n == AT_STATS + 1:
                        root(2 * (c + 1))
                    if c + 1 < CHUNKS and n == AT_PV + 1:
                        root(2 * (c + 1) + 1)
                    low_part(c, n)

        @block.scalar
        def _(sc):
            sc.dma_start(router_sb[:, :], router).then_inc(router_loaded, 16)
            sc.dma_start(tok_sb[:, :, :], token_sets.rearrange("(h p) k -> p h k", p=P)).then_inc(small_loaded, 16)
            sc.dma_start(bq_sb[:, :], b_q.rearrange("(k p) -> p k", p=P), allow_slow_non_contiguous=True).then_inc(small_loaded, 16)
            for i, g in enumerate((g_xattn, g_ffn)):
                sc.dma_start(gates_in[:, i:i + 1],
                             g.rearrange("(a b) -> a b", a=1).to_broadcast([P, 1])).then_inc(small_loaded, 16)
            for m, src in ((0, gate_scales), (1, up_scales)):
                sc.dma_start(scales_sb[:, :, m * D // BLK:(m + 1) * D // BLK],
                             src.rearrange("(u p) b -> p u b", p=P)).then_inc(scales_loaded, 16)
            q = P // BLK
            for a in range(KT):
                at = 2 * D // BLK + a * q
                sc.dma_start(scales_sb[:, :, at:at + q],
                             down_scales[a * P:(a + 1) * P, :].rearrange("p (u b) -> p u b", b=q)).then_inc(scales_loaded, 16)

            sc.wait_ge(router_turned, 1)
            sc.activation(router_t[:, :, :], acc_ps[:, 0, 0:KT * SETS].rearrange("p (k n) -> p k n", k=KT),
                          ACT.Copy).then_inc(router_copied, 1)
            sc.wait_ge(small_loaded, 16 * 4)
            sc.activation(gates[:, :], gates_in[:, :], ACT.Tanh).then_inc(gates_ready, 1)
            sc.wait_ge(score_w_done, 1)
            sc.activation(score_w[:, :, :], acc_ps[:, 1, 0:KT * SETS].rearrange("p (k n) -> p k n", k=KT),
                          ACT.Copy).then_inc(score_w_copied, 1)

            def unit_high(u):
                sc.wait_ge(unit_turned, u + 1)
                for b in range(2):
                    sc.activation(w_hi[:, u, b * WU // 2:(b + 1) * WU // 2], turned_unit(u)[:, b, 0:WU // 2],
                                  ACT.Copy, scale=FP4_SHIFT).then_inc(hi_stored, 1)

            def ln1_out(c):
                sc.wait_ge(ln1_turned, c + 1)
                if c >= 2:
                    sc.wait_ge(out_turned, c - 1)
                for k in range(KT):
                    sc.activation(turned[:, k, :], misc_ps[:, k, :], ACT.Copy).then_inc(ln1_copied, 1)

            def second_weight(c):
                sc.wait_ge(gap_ready, c + 1)
                sc.activation(second[:, :], gap[:, :], ACT.Exp).then_inc(second_ready, 1)

            def probs_out(c):
                sc.wait_ge(probs_turned, c + 1)
                sc.activation(probs_t[:, :], misc_ps[0:SETS, 0, :], ACT.Copy).then_inc(probs_copied, 1)

            def ln2_high(c):
                sc.wait_ge(ln2_turned, c + 1)
                for k in range(KT):
                    sc.activation(xt_hi[:, c, k, :], misc_ps[:, k, :], ACT.Copy).then_inc(xt_hi_ready, 1)

            def acc_out(c):
                sc.wait_ge(down_done, UNITS * (c + 1))
                if c + 1 < CHUNKS:
                    sc.wait_ge(scores_done, c + 2)
                for a in range(KT):
                    sc.activation(turned[:, a, :], acc_ps[:, a, :], ACT.Copy, scale=gates[:, 1:2]).then_inc(acc_copied, 1)

            def square(c, n):
                s = c * UNITS + n
                sc.wait_ge(gate_done, s + 1)
                if c > 0 or n >= 2:
                    sc.wait_ge(inter_lo, s - 1)
                sc.activation(act[:, n % 2, :], gate_ps[:, n % 2, :], ACT.Square).then_inc(squared, 1)

            def tanh(c, n):
                s = c * UNITS + n
                sc.wait_ge(cubic_done, s + 1)
                sc.activation(act[:, n % 2, :], act[:, n % 2, :], ACT.Tanh,
                              scale=GELU_SCALE * GELU_CUBIC).then_inc(tanh_done, 1)

            def high_part(c, n):
                s = c * UNITS + n
                sc.wait_ge(inter_done, s + 1)
                if c > 0 or n >= RING:
                    sc.wait_ge(down_done, s - RING + 1)
                sc.activation(act_hi[:, n % RING, :], act[:, n % 2, :], ACT.Copy).then_inc(inter_hi, 1)

            ln1_out(0)
            unit_high(0)
            second_weight(0)
            probs_out(0)
            unit_high(1)
            ln2_high(0)
            for c in range(CHUNKS):
                for n in range(UNITS):
                    square(c, n)
                    if c == 0 and LEAD <= n + 1 < UNITS:
                        unit_high(n + 1)
                    tanh(c, n)
                    if c + 1 < CHUNKS:
                        if n == AT_LN1:
                            ln1_out(c + 1)
                        if n == AT_WEIGHTS:
                            second_weight(c + 1)
                        if n == AT_PT:
                            probs_out(c + 1)
                        if n == AT_LN2:
                            ln2_high(c + 1)
                    high_part(c, n)
                    if c > 0 and n == 1:
                        acc_out(c - 1)
            acc_out(CHUNKS - 1)

        @block.vector
        def _(dve):
            chain = [0]

            def link(ins):
                chain[0] += 1
                ins.then_inc(attn, 1)
                dve.wait_ge(attn, chain[0])

            def layer_stats(n, c):
                for t in range(CT):
                    i = dve.bn_stats(stats[:, t, :], x_sb[:, c * CT + t, :])
                link(i)
                for t in range(CT):
                    i = dve.bn_aggr(mean_var[:, t, :], stats[:, t, :])
                link(i)
                if n > 0:
                    dve.wait_ge(rstd_ready, n)
                dve.tensor_scalar(var_eps[:, :], mean_var[:, :, 1], LN_EPS, None, ALU.add).then_inc(var_ready, 1)

            def stats_1(c):
                if c == 0:
                    dve.wait_ge(x_loaded, 16)
                else:
                    dve.wait_ge(x_rest_loaded, 16)
                layer_stats(2 * c, c)

            def stats_2(c):
                dve.wait_ge(x_updated, 2 * (c + 1))
                layer_stats(2 * c + 1, c)

            def normalise(n, c):
                dve.wait_ge(rstd_ready, n + 1)
                if n % 2:
                    dve.wait_ge(ln1_turned, c + 1)
                elif n > 0:
                    dve.wait_ge(ln2_turned, c)
                for t in range(CT):
                    i = dve.tensor_scalar(normed[:, t, :], x_sb[:, c * CT + t, :], mean_var[:, t, 0:1],
                                          rstd[:, t:t + 1], ALU.subtract, ALU.mult)
                i.then_inc(normed_ready, 1)

            def pick(c):
                dve.wait_ge(scores_done, c + 1)
                dve.scalar_tensor_tensor(
                    scores[:, :, :].rearrange("p (b h) n -> p b (h n)", h=HALVES),
                    misc_ps[:, 0, 0:CT * SETS].rearrange("p (b m) -> p b m", b=CB), SCORE_SCALE,
                    score_bias[:, :, :].rearrange("p h n -> p (h n)").unsqueeze(1).to_broadcast([P, CB, HALVES * SETS]),
                    ALU.mult, ALU.add).then_inc(scores_read, 1)
                dve.wait_ge(scores_read, c + 1)
                for t in range(CT):
                    i = dve.max(top8[:, t, :], scores[:, t, :])
                link(i)
                if c > 0:
                    dve.wait_ge(second_ready, c)
                dve.tensor_tensor(gap[:, :], top8[:, :, 1], top8[:, :, 0], ALU.subtract).then_inc(gap_ready, 1)
                for t in range(CT):
                    i = dve.max_index(top8_at[:, t, :], top8[:, t, :], scores[:, t, :])
                link(i)
                link(dve.tensor_copy(top2_at[:, :, :], top8_at[:, :, 0:2]))

            def weigh(c):
                dve.wait_ge(second_ready, c + 1)
                link(dve.tensor_scalar(total[:, :], second[:, :], 1.0, None, ALU.add))
                link(dve.reciprocal(inv_total[:, :], total[:, :]))
                if c == 0:
                    dve.wait_ge(gates_ready, 1)
                link(dve.tensor_scalar(w_first[:, :], inv_total[:, :], gates[:, 0:1], None, ALU.mult))
                link(dve.tensor_tensor(w_second[:, :], w_first[:, :], second[:, :], ALU.mult))
                for t in range(CT):
                    dve.tensor_scalar(probs_a[:, t, :], iota_f[:, :], top2_at[:, t, 0:1], w_first[:, t:t + 1],
                                      ALU.is_equal, ALU.mult)
                    i = dve.tensor_scalar(probs_b[:, t, :], iota_f[:, :], top2_at[:, t, 1:2], w_second[:, t:t + 1],
                                          ALU.is_equal, ALU.mult)
                link(i)
                dve.tensor_tensor(probs[:, :, :], probs_a[:, :, :], probs_b[:, :, :], ALU.add).then_inc(probs_ready, 1)

            def tiles(c, b):
                t = c * CT + b * HALVES
                return x_sb[:, t:t + HALVES, :].rearrange("p t d -> p (t d)")

            def add_attention(c):
                dve.wait_ge(attended, c + 1)
                for b in range(2):
                    dve.tensor_tensor(tiles(c, b), misc_ps[:, b, :], tiles(c, b), ALU.add).then_inc(x_updated, 1)

            def ln2_low(c):
                dve.wait_ge(xt_hi_ready, 2 * (c + 1))
                for k in range(KT):
                    dve.tensor_tensor(xt_lo[:, c, k, :], misc_ps[:, k, :], xt_hi[:, c, k, :].bitcast(F32),
                                      ALU.subtract).then_inc(xt_lo_ready, 1)

            def add_output(c):
                dve.wait_ge(out_turned, c + 1)
                for b in range(2):
                    dve.tensor_tensor(tiles(c, b), misc_ps[:, b, :], tiles(c, b), ALU.add).then_inc(out_ready, 1)

            bits = [0]

            def unpack(u):
                if u % PG == 0:
                    dve.wait_ge(packed_loaded[u // PG], 16 * 4)
                words = packed[:, u % PRING, :]

                def then(ins):
                    bits[0] += 1
                    ins.then_inc(lined_up, 1)
                    dve.wait_ge(lined_up, bits[0])

                then(dve.tensor_scalar(high_codes[:, :], words, 0xF0, 12, ALU.bitwise_and, ALU.logical_shift_left))
                then(dve.scalar_tensor_tensor(words, words, 0xF, high_codes[:, :], ALU.bitwise_and, ALU.bitwise_or))
                then(dve.scalar_tensor_tensor(words, words, 3, words, ALU.logical_shift_left, ALU.bitwise_or))
                if u > 0:
                    dve.wait_ge(scaled, u)
                dve.tensor_scalar(code_bits[:, :], words, 9, FP4_MASK, ALU.logical_shift_left,
                                  ALU.bitwise_and).then_inc(unpacked, 1)

            def unit_low(u):
                dve.wait_ge(hi_stored, 2 * (u + 1))
                for b in range(2):
                    part = slice(b * WU // 2, (b + 1) * WU // 2)
                    dve.scalar_tensor_tensor(w_lo[:, u, part], turned_unit(u)[:, b, 0:WU // 2], FP4_SHIFT,
                                             w_hi[:, u, part].bitcast(F32), ALU.mult,
                                             ALU.subtract).then_inc(lo_stored, 1)

            def cubic(c, n):
                s = c * UNITS + n
                dve.wait_ge(squared, s + 1)
                a = act[:, n % 2, :]
                dve.scalar_tensor_tensor(a, a, 1.0 / GELU_CUBIC, gate_ps[:, n % 2, :], ALU.add,
                                         ALU.mult).then_inc(cubic_done, 1)

            def gelu(c, n):
                s = c * UNITS + n
                dve.wait_ge(tanh_done, s + 1)
                a = act[:, n % 2, :]
                dve.scalar_tensor_tensor(a, a, 1.0, gate_ps[:, n % 2, :], ALU.add, ALU.mult).then_inc(gelu_done, 1)

            def times_up(c, n):
                s = c * UNITS + n
                dve.wait_ge(up_done, s + 1)
                dve.wait_ge(gelu_done, s + 1)
                a = act[:, n % 2, :]
                dve.scalar_tensor_tensor(a, a, 0.5, up_ps[:, n % 2, :], ALU.mult, ALU.mult).then_inc(inter_done, 1)

            step = [0]

            def setup_link(ins):
                step[0] += 1
                ins.then_inc(setup, 1)
                dve.wait_ge(setup, step[0])

            stats_1(0)
            dve.wait_ge(small_loaded, 16 * 4)
            dve.tensor_copy(bq_wide[:, :, :], bq_sb[:, :].unsqueeze(2).to_broadcast([P, KT, P])).then_inc(bq_spread, 1)
            setup_link(dve.tensor_copy(tok_f[:, :, :], tok_sb[:, :, :]))
            dve.wait_ge(iota_made, 1)
            setup_link(dve.tensor_copy(iota_f[:, :], iota_i[:, :]))
            normalise(0, 0)
            for k in range(PICKS):
                for h in range(HALVES):
                    pick_k = tok_f[:, h, k:k + 1]
                    if k == 0:
                        i = dve.tensor_scalar(allowed[:, h, :], iota_f[:, :], pick_k, None, ALU.is_equal)
                    else:
                        i = dve.scalar_tensor_tensor(allowed[:, h, :], iota_f[:, :], pick_k, allowed[:, h, :],
                                                     ALU.is_equal, ALU.add)
                setup_link(i)
            setup_link(dve.tensor_scalar(allowed[:, :, :], allowed[:, :, :], 0.5, MASKED, ALU.is_lt, ALU.mult))
            unpack(0)
            dve.wait_ge(score_w_copied, 1)
            cb = acc_ps[:, 1, KT * SETS:(KT + 1) * SETS].unsqueeze(1).to_broadcast([P, HALVES, SETS])
            setup_link(dve.scalar_tensor_tensor(score_bias[:, :, :], cb, SCORE_SCALE, allowed[:, :, :],
                                                ALU.mult, ALU.add))
            pick(0)
            unpack(1)
            weigh(0)
            unit_low(0)
            unpack(2)
            add_attention(0)
            stats_2(0)
            unit_low(1)
            normalise(1, 0)
            ln2_low(0)
            for c in range(CHUNKS):
                nxt = c + 1 < CHUNKS
                for n in range(UNITS):
                    cubic(c, n)
                    if c == 0 and LEAD <= n + 1 < UNITS:
                        unit_low(n + 1)
                    gelu(c, n)
                    if nxt and n == AT_SCORES:
                        pick(c + 1)
                    if nxt and n == AT_PV:
                        add_attention(c + 1)
                    if nxt and n == AT_LN2:
                        ln2_low(c + 1)
                    if c > 0 and n == AT_OUT:
                        add_output(c - 1)
                    times_up(c, n)
                    if c == 0 and n + DECODE_LEAD < UNITS:
                        unpack(n + DECODE_LEAD)
                    if nxt and n == AT_STATS:
                        stats_1(c + 1)
                    if nxt and n == AT_NORM:
                        normalise(2 * (c + 1), c + 1)
                    if nxt and n == AT_WEIGHTS:
                        weigh(c + 1)
                    if nxt and n == AT_PV:
                        stats_2(c + 1)
                    if nxt and n == AT_NORM2:
                        normalise(2 * (c + 1) + 1, c + 1)
            add_output(CHUNKS - 1)

        @block.tensor
        def _(pe):
            def turn_router():
                pe.wait_ge(ident_made, 2)
                pe.wait_ge(router_loaded, 16)
                for k in range(KT):
                    i = pe.transpose(acc_ps[:, 0, k * SETS:(k + 1) * SETS], router_sb[:, k * P:(k + 1) * P],
                                     ident[0:SETS, 0:SETS])
                i.then_inc(router_turned, 1)

            def fold_router():
                pe.wait_ge(router_copied, 1)
                pe.wait_ge(wq_loaded, 16)
                for k in range(KT):
                    for e in range(KT):
                        pe.matmul(acc_ps[:, 1, k * SETS:(k + 1) * SETS], wq_sb[:, e, k * P:(k + 1) * P],
                                  router_t[:, e, :], start=(e == 0), stop=(e == KT - 1))
                pe.wait_ge(bq_spread, 1)
                for e in range(KT):
                    i = pe.matmul(acc_ps[:, 1, KT * SETS:(KT + 1) * SETS], bq_wide[:, e, :], router_t[:, e, :],
                                  start=(e == 0), stop=(e == KT - 1))
                i.then_inc(score_w_done, 1)

            def turn_normed(n, done):
                pe.wait_ge(normed_ready, n + 1)
                for k in range(KT):
                    for t in range(CT):
                        i = pe.transpose(misc_ps[:, k, t * P:(t + 1) * P], normed[:, t, k * P:(k + 1) * P], ident[:, :])
                i.then_inc(done, 1)

            def score(c):
                pe.wait_ge(ln1_copied, 2 * (c + 1))
                if c == 0:
                    pe.wait_ge(score_w_copied, 1)
                for t in range(CT):
                    for k in range(KT):
                        i = pe.matmul(misc_ps[:, 0, t * SETS:(t + 1) * SETS], turned[:, k, t * P:(t + 1) * P],
                                      score_w[:, k, :], start=(k == 0), stop=(k == KT - 1))
                i.then_inc(scores_done, 1)

            def turn_probs(c):
                pe.wait_ge(probs_ready, c + 1)
                for t in range(CT):
                    i = pe.transpose(misc_ps[0:SETS, 0, t * P:(t + 1) * P], probs[:, t, :], ident[:, :])
                i.then_inc(probs_turned, 1)

            def attend(c):
                pe.wait_ge(probs_copied, c + 1)
                if c == 0:
                    pe.wait_ge(ctx_loaded, 16)
                for t in range(CT):
                    i = pe.matmul(misc_ps[:, t // 2, (t % 2) * D:(t % 2 + 1) * D], probs_t[:, t * P:(t + 1) * P],
                                  ctx_sb[:, c * CB + t // HALVES, :], start=True, stop=True)
                i.then_inc(attended, 1)

            def turn_unit(u):
                pe.wait_ge(scaled, u + 1)
                for i6 in range(WU // P):
                    b, at = divmod(i6 * P, WU // 2)
                    i = pe.transpose(turned_unit(u)[:, b, at:at + P], w_nat[:, u % 2, i6 * P:(i6 + 1) * P], ident[:, :])
                i.then_inc(unit_turned, 1)

            def unit_copied(u):
                pe.wait_ge(hi_stored, 2 * (u + 1))
                pe.wait_ge(lo_stored, 2 * (u + 1))

            def project(c, n, m, into, done):
                first, last = True, (KT - 1, 2)
                for k in range(KT):
                    w = slice(m * D + k * P, m * D + (k + 1) * P)
                    for j, (wt, xt) in enumerate(((w_hi, xt_hi), (w_hi, xt_lo), (w_lo, xt_hi))):
                        i = pe.matmul(into, wt[:, n, w], xt[:, c, k, :], start=first, stop=(k, j) == last)
                        first = False
                i.then_inc(done, 1)

            def down(c, n):
                s = c * UNITS + n
                pe.wait_ge(inter_hi, s + 1)
                if n == 0 and c > 0:
                    pe.wait_ge(acc_copied, 2 * c)
                for part in range(3):
                    if part == 2:
                        pe.wait_ge(inter_lo, s + 1)
                    for a in range(KT):
                        wt = w_lo if part == 1 else w_hi
                        h = act_lo[:, n % 2, :] if part == 2 else act_hi[:, n % RING, :]
                        i = pe.matmul(acc_ps[:, a, :], wt[:, n, 2 * D + a * P:2 * D + (a + 1) * P], h,
                                      start=(n == 0 and part == 0), stop=(n == UNITS - 1 and part == 2))
                i.then_inc(down_done, 1)

            def turn_output(c):
                pe.wait_ge(acc_copied, 2 * (c + 1))
                for t in range(CT):
                    for a in range(KT):
                        at = (t % 2) * D + a * P
                        i = pe.transpose(misc_ps[:, t // 2, at:at + P], turned[:, a, t * P:(t + 1) * P], ident[:, :])
                i.then_inc(out_turned, 1)

            turn_router()
            fold_router()
            turn_normed(0, ln1_turned)
            turn_unit(0)
            score(0)
            turn_unit(1)
            turn_probs(0)
            attend(0)
            turn_normed(1, ln2_turned)

            for c in range(CHUNKS):
                nxt = c + 1 < CHUNKS
                pe.wait_ge(xt_hi_ready, 2 * (c + 1))
                pe.wait_ge(xt_lo_ready, 2 * (c + 1))
                for n in range(UNITS):
                    s = c * UNITS + n
                    if c == 0:
                        unit_copied(n)
                    if c > 0 or n >= 2:
                        pe.wait_ge(gelu_done, s - 1)
                    project(c, n, 0, gate_ps[:, n % 2, :], gate_done)
                    if c == 0 and n == 0:
                        unit_copied(1)
                    if c > 0 or n >= 2:
                        pe.wait_ge(inter_done, s - 1)
                    project(c, n, 1, up_ps[:, n % 2, :], up_done)

                    if c > 0 and n == AT_OUT:
                        turn_output(c - 1)
                    if nxt and n in (AT_LN1, AT_SCORES, AT_PT, AT_PV, AT_LN2):
                        if c == 0:
                            unit_copied(n + LEAD - 1)
                        if n == AT_LN1:
                            if c > 0:
                                pe.wait_ge(out_ready, 2 * c)
                            turn_normed(2 * (c + 1), ln1_turned)
                        elif n == AT_SCORES:
                            score(c + 1)
                        elif n == AT_PT:
                            turn_probs(c + 1)
                        elif n == AT_PV:
                            attend(c + 1)
                        else:
                            turn_normed(2 * (c + 1) + 1, ln2_turned)

                    if c > 0 or n >= 2:
                        down(*((c, n - 2) if n >= 2 else (c - 1, UNITS + n - 2)))

                    if c == 0 and n + LEAD < UNITS:
                        if n == 0:
                            pe.wait_ge(xt_lo_ready, 2)
                        else:
                            unit_copied(n + LEAD - 1)
                        if n == AT_LN1:
                            pe.wait_ge(ln1_copied, 4)
                        if n == AT_SCORES:
                            pe.wait_ge(scores_read, 2)
                        if n == AT_PT:
                            pe.wait_ge(probs_copied, 2)
                        if n == AT_PV:
                            pe.wait_ge(x_updated, 4)
                        if n == AT_LN2:
                            pe.wait_ge(xt_hi_ready, 4)
                            pe.wait_ge(xt_lo_ready, 4)
                        turn_unit(n + LEAD)
            down(CHUNKS - 1, UNITS - 2)
            down(CHUNKS - 1, UNITS - 1)
            turn_output(CHUNKS - 1)


_INS = ["x", "ctx_2048", "itok_Sx4_0_63", "g_xattn", "g_ffn", "L0_xattn_desc_router", "L0_xattn_W_q", "L0_xattn_b_q",
        "L0_ffn_gate_W_packed", "L0_ffn_gate_scales", "L0_ffn_up_W_packed", "L0_ffn_up_scales",
        "L0_ffn_down_W_packed", "L0_ffn_down_scales"]
_OUTS = [((8, 256, 256), "float32")]


def kernel(**inputs):
    import numpy as _np
    import concourse.bacc as _bacc
    from concourse import mybir as _mybir
    from concourse.bass_utils import run_bass_kernel_spmd as _run

    nc = _bacc.Bacc("TRN2", target_bir_lowering=False, num_devices=1)
    arrays, args = {}, []
    for name in _INS:
        a = _np.ascontiguousarray(inputs[name])
        arrays[f"in_{name}_dram"] = a
        args.append(nc.dram_tensor(f"in_{name}_dram", a.shape, _mybir.dt.from_np(a.dtype), kind="ExternalInput").ap())
    for i, (shape, dtype) in enumerate(_OUTS):
        dt = _mybir.dt.from_np(_np.dtype(dtype))
        args.append(nc.dram_tensor(f"out_{i}_dram", shape, dt, kind="ExternalOutput").ap())
    build_program(nc, *args)
    r = _run(nc, [arrays], core_ids=[0])
    got = tuple(r.results[0][f"out_{i}_dram"] for i in range(len(_OUTS)))
    return got[0]
```

```python
from contextlib import ExitStack

import concourse.bass as bass
from concourse import mybir

ALU = mybir.AluOpType
ACT = mybir.ActivationFunctionType
F32 = mybir.dt.float32
F32R = mybir.dt.float32r
I32 = mybir.dt.int32
U32 = mybir.dt.uint32
U8 = mybir.dt.uint8
F8E5 = mybir.dt.float8e5

P = 128
LN_EPS = 1e-5
MASKED = -3.0e38
GELU_CUBIC = 0.044715
GELU_SCALE = 0.7978845608028654
LOW_NIBBLES = 0x0F0F0F0F
CODE_BITS = 0x8E8E8E8E - (1 << 32)
FP4_SHIFT = 16384.0


def build_program(
    nc: bass.Bass,
    x: bass.AP,
    ctx_sets: bass.AP,
    token_sets: bass.AP,
    g_xattn: bass.AP,
    g_ffn: bass.AP,
    router: bass.AP,
    w_q: bass.AP,
    b_q: bass.AP,
    gate_packed: bass.AP,
    gate_scales: bass.AP,
    up_packed: bass.AP,
    up_scales: bass.AP,
    down_packed: bass.AP,
    down_scales: bass.AP,
    out: bass.AP,
):
    BATCH, SEQ, D = x.shape
    SETS = ctx_sets.shape[1]
    PICKS = token_sets.shape[1]
    MLP = gate_packed.shape[0]
    KT = D // P
    TILES = BATCH * SEQ // P
    CT = 4
    CHUNKS = TILES // CT
    TOK = CT * P
    HALVES = SEQ // P
    CB = CT // HALVES
    ST = HALVES * P
    UNITS = MLP // P
    CODES = 3 * D // 2
    WU = 3 * D
    BLK = 32
    SU = WU // BLK
    PG = 2
    PRING = 4
    RING = 2
    SCORE_SCALE = float(D) ** -0.5
    assert KT == 2 and HALVES == 2 and UNITS % RING == 0 and down_packed.shape[0] == D

    LEAD = 2
    DECODE_LEAD = 3
    COMPACT_LEAD = 4
    LAG = 2

    (STATS_1, CENTER_1, TURN_1, SCORE, WEIGH, SPREAD, TURN_PROBS, ATTEND, STATS_2, CENTER_2,
     TURN_2) = range(11)
    SEQ_BEGIN = (0, 4)
    AT_OUT = (12, 15)

    x_v = x.rearrange("b (h p) d -> p (b h) d", p=P)
    out_v = out.rearrange("b (h p) d -> p (b h) d", p=P)
    ctx_v = ctx_sets.rearrange("b n d -> n b d")

    with ExitStack() as stack:
        def sb(name, shape, dt=F32):
            return stack.enter_context(nc.sbuf_tensor(name, shape, dt))

        def psum(name, shape):
            return stack.enter_context(nc.psum_tensor(name, shape, F32))

        def sem(name):
            return stack.enter_context(nc.semaphore(name))

        x_sb = sb("x_sb", [P, TILES, D])
        ctx_sb = sb("ctx_sb", [SETS, BATCH, D])
        tok_sb = sb("tok_sb", [P, HALVES, PICKS], I32)
        router_sb = sb("router_sb", [SETS, D])
        bq_sb = sb("bq_sb", [P, KT])
        router_t = sb("router_t", [P, KT, SETS])
        score_w = sb("score_w", [P, KT, SETS])
        iota_i = sb("iota_i", [P, SETS], I32)
        iota_f = sb("iota_f", [P, SETS])
        allowed = sb("allowed", [P, HALVES, SETS])
        score_bias = sb("score_bias", [P, HALVES, SETS])
        gates_in = sb("gates_in", [P, 2])
        gates = sb("gates", [P, 2])
        half_gate = sb("half_gate", [P, 2])
        ident = sb("ident", [P, P])
        minus_half = sb("minus_half", [P, HALVES])

        stats = sb("stats", [P, CB, HALVES, 6])
        mean_var = sb("mean_var", [P, CB, HALVES, 2])
        var_eps = sb("var_eps", [P, CB, HALVES])
        rstd = sb("rstd", [P, CB, HALVES])
        shift = sb("shift", [P, CB, HALVES])
        normed = sb("normed", [P, CB, HALVES, D])
        ln1_t = sb("ln1_t", [P, CB, KT, ST])
        scores = sb("scores", [P, CB, HALVES, SETS])
        top8 = sb("top8", [P, CB, HALVES, 8])
        top8_at = sb("top8_at", [P, CB, HALVES, 8], U32)
        top2_at = sb("top2_at", [P, CB, HALVES, 2])
        lead = sb("lead", [P, CB, HALVES])
        lead_tanh = sb("lead_tanh", [P, CB, HALVES])
        w_first = sb("w_first", [P, CB, HALVES])
        w_second = sb("w_second", [P, CB, HALVES])
        probs_a = sb("probs_a", [P, HALVES, SETS])
        probs_b = sb("probs_b", [P, HALVES, SETS])
        probs = sb("probs", [P, CB, HALVES, SETS])
        probs_t = sb("probs_t", [SETS, CB, ST])
        out_t = sb("out_t", [P, KT, TOK])

        packed = sb("packed", [P, PRING, CODES], I32)
        scales_sb = sb("scales_sb", [P, UNITS, SU])
        code_bytes = sb("code_bytes", [P, 2, CODES // 4], I32)
        nibbles = sb("nibbles", [P, WU // P, 2, P // 8], I32)
        code_bits = sb("code_bits", [P, 2, WU // 4], I32)
        w_nat = sb("w_nat", [P, 2, WU])
        w_hi = sb("w_hi", [P, UNITS, WU], F32R)
        w_lo = sb("w_lo", [P, UNITS, WU], F32R)
        xt_hi = sb("xt_hi", [P, CHUNKS, KT, TOK], F32R)
        xt_lo = sb("xt_lo", [P, CHUNKS, KT, TOK], F32R)
        act = sb("act", [P, RING, TOK])
        half_gu = sb("half_gu", [P, 2, TOK])
        wq_sb = half_gu[:, 0, :].rearrange("p (k d) -> p k d", k=KT)
        bq_wide = half_gu[:, 1, 0:KT * P].rearrange("p (k e) -> p k e", k=KT)
        hits = act[:, 0, :].rearrange("p (k h n) -> p k h n", k=PICKS, h=HALVES)
        act_hi = sb("act_hi", [P, RING, TOK], F32R)
        act_lo = sb("act_lo", [P, 2, TOK], F32R)

        gate_ps = psum("gate_ps", [P, 2, TOK])
        up_ps = psum("up_ps", [P, 2, TOK])
        acc_ps = psum("acc_ps", [P, KT, TOK])
        misc_ps = psum("misc_ps", [P, 2, TOK])

        x_loaded = [sem(f"x_loaded{b}") for b in range(CB)]
        x_rest_loaded = sem("x_rest_loaded")
        ctx_loaded = sem("ctx_loaded")
        ctx_rest_loaded = sem("ctx_rest_loaded")
        router_loaded = sem("router_loaded")
        small_loaded = sem("small_loaded")
        wq_loaded = sem("wq_loaded")
        scales_loaded = sem("scales_loaded")
        scales_rest_loaded = sem("scales_rest_loaded")
        packed_loaded = [sem(f"packed_loaded{g}") for g in range(UNITS // PG)]
        stored = sem("stored")

        ident_made = sem("ident_made")
        iota_made = sem("iota_made")
        minus_half_made = sem("minus_half_made")
        tokens_loaded = sem("tokens_loaded")
        mask_made = sem("mask_made")
        bq_spread = sem("bq_spread")
        router_turned = sem("router_turned")
        router_copied = sem("router_copied")
        score_w_done = sem("score_w_done")
        score_w_copied = sem("score_w_copied")
        gates_ready = sem("gates_ready")

        compacted = sem("compacted")
        lined_up = sem("lined_up")
        unpacked = sem("unpacked")
        scaled = sem("scaled")
        unit_turned = sem("unit_turned")
        hi_stored = sem("hi_stored")
        lo_stored = sem("lo_stored")

        attn = sem("attn")
        var_ready = sem("var_ready")
        rstd_ready = sem("rstd_ready")
        shift_ready = sem("shift_ready")
        normed_ready = sem("normed_ready")
        ln1_turned = sem("ln1_turned")
        ln1_copied = sem("ln1_copied")
        scores_done = sem("scores_done")
        scores_read = sem("scores_read")
        lead_ready = sem("lead_ready")
        lead_tanh_ready = sem("lead_tanh_ready")
        probs_ready = sem("probs_ready")
        probs_turned = sem("probs_turned")
        probs_copied = sem("probs_copied")
        attended = sem("attended")
        x_updated = sem("x_updated")
        ln2_turned = sem("ln2_turned")
        xt_hi_ready = sem("xt_hi_ready")
        xt_lo_ready = sem("xt_lo_ready")

        gate_done = sem("gate_done")
        up_done = sem("up_done")
        cubic_done = sem("cubic_done")
        tanh_done = sem("tanh_done")
        halved = sem("halved")
        gated_up = sem("gated_up")
        inter_done = sem("inter_done")
        inter_hi = sem("inter_hi")
        inter_lo = sem("inter_lo")
        down_done = sem("down_done")
        acc_copied = sem("acc_copied")
        out_turned = sem("out_turned")
        out_ready = sem("out_ready")

        def turned_unit(u):
            return (gate_ps, up_ps, misc_ps)[min(u, LEAD)]

        def next_sequences(c, n, stage):
            return [(c + 1) * CB + i for i in range(CB) if c + 1 < CHUNKS and n == SEQ_BEGIN[i] + stage]

        LN_COUNT = {(0, 0): 1, (1, 0): 2, (0, 1): 3, (1, 1): 4}
        for c in range(CHUNKS):
            for n in range(UNITS):
                for ln, stage in ((0, STATS_1), (1, STATS_2)):
                    for b in next_sequences(c, n, stage):
                        LN_COUNT[b, ln] = len(LN_COUNT) + 1

        block = stack.enter_context(nc.Block())

        @block.sync
        def _(sp):
            def load_x(b0, b1, done):
                t = slice(b0 * HALVES, b1 * HALVES)
                sp.dma_start(x_sb[:, t, :], x_v[:, t, :]).then_inc(done, 16)

            def load_packed(g):
                at = g * PG % PRING
                ring = slice(at, at + PG)
                units = slice(g * PG * P, (g + 1) * PG * P)
                if g * PG >= PRING:
                    sp.wait_ge(compacted, (g + 1) * PG - PRING)
                for m, src in ((0, gate_packed), (1, up_packed)):
                    sp.dma_start(packed[:, ring, m * P:(m + 1) * P],
                                 src[units, :].rearrange("(u p) j -> p u j", p=P)).then_inc(packed_loaded[g], 16)
                half = P // 2
                for a in range(KT):
                    sp.dma_start(packed[:, ring, 2 * P + a * half:2 * P + (a + 1) * half],
                                 down_packed[a * P:(a + 1) * P, g * PG * half:(g + 1) * PG * half]
                                 .rearrange("p (u j) -> p u j", u=PG)).then_inc(packed_loaded[g], 16)

            def load_scales(u0, u1, done):
                rows = slice(u0 * P, u1 * P)
                for m, src in ((0, gate_scales), (1, up_scales)):
                    sp.dma_start(scales_sb[:, u0:u1, m * D // BLK:(m + 1) * D // BLK],
                                 src[rows, :].rearrange("(u p) b -> p u b", p=P)).then_inc(done, 16)
                q = P // BLK
                for a in range(KT):
                    at = 2 * D // BLK + a * q
                    sp.dma_start(scales_sb[:, u0:u1, at:at + q],
                                 down_scales[a * P:(a + 1) * P, u0 * q:u1 * q]
                                 .rearrange("p (u b) -> p u b", b=q)).then_inc(done, 16)

            load_x(0, 1, x_loaded[0])
            load_x(1, 2, x_loaded[1])
            sp.dma_start(bq_sb[:, :], b_q.rearrange("(k p) -> p k", p=P),
                         allow_slow_non_contiguous=True).then_inc(small_loaded, 16)
            for i, g in enumerate((g_xattn, g_ffn)):
                sp.dma_start(gates_in[:, i:i + 1],
                             g.rearrange("(a b) -> a b", a=1).to_broadcast([P, 1])).then_inc(small_loaded, 16)
            load_packed(0)
            load_scales(0, PRING, scales_loaded)
            sp.dma_start(ctx_sb[:, 0:CB, :], ctx_v[:, 0:CB, :]).then_inc(ctx_loaded, 16)
            load_packed(1)
            load_scales(PRING, UNITS, scales_rest_loaded)
            load_x(CB, BATCH, x_rest_loaded)
            sp.dma_start(ctx_sb[:, CB:BATCH, :], ctx_v[:, CB:BATCH, :]).then_inc(ctx_rest_loaded, 16)
            for g in range(PRING // PG, UNITS // PG):
                load_packed(g)
            for b in range(2 * CHUNKS):
                sp.wait_ge(out_ready, b + 1)
                t = slice(b * HALVES, (b + 1) * HALVES)
                sp.dma_start(out_v[:, t, :], x_sb[:, t, :]).then_inc(stored, 16)
            sp.wait_ge(stored, 16 * 2 * CHUNKS)

        @block.gpsimd
        def _(pool):
            pool.dma_start(tok_sb[:, :, :], token_sets.rearrange("(h p) k -> p h k", p=P)).then_inc(tokens_loaded, 16)
            pool.memset(ident[:, :], 0.0).then_inc(ident_made, 1)
            pool.iota(iota_i[:, :], [[1, SETS]], base=0, channel_multiplier=0).then_inc(iota_made, 1)
            pool.wait_ge(ident_made, 1)
            pool.affine_select(out=ident[:, :], in_=ident[:, :], compare_op=ALU.not_equal, fill=1.0, base=0,
                               pattern=[[-1, P]], channel_multiplier=1).then_inc(ident_made, 1)
            pool.memset(minus_half[:, :], -0.5).then_inc(minus_half_made, 1)

            pool.wait_ge(mask_made, 1)
            pool.tensor_tensor(hits[:, 0:2], hits[:, 0:2], hits[:, 2:4], ALU.add).then_inc(mask_made, 1)

            def scale_unit(u):
                if u == 0:
                    pool.wait_ge(scales_loaded, 16 * 4)
                if u == PRING:
                    pool.wait_ge(scales_rest_loaded, 16 * 4)
                pool.wait_ge(unpacked, u + 1)
                if u >= 2:
                    pool.wait_ge(unit_turned, u - 1)
                q = P // BLK
                codes = code_bits[:, u % 2, :].bitcast(F8E5).rearrange("p (g i b k) -> p g i b k", i=2, b=q, k=BLK // 2)
                w = w_nat[:, u % 2, :].rearrange("p (g i b k) -> p g i b k", i=2, b=q, k=BLK // 2)
                s = (scales_sb[:, u, :].rearrange("p (g b) -> p g b", b=q).unsqueeze(3)
                     .to_broadcast([P, WU // P, q, BLK // 2]))
                for i in range(2):
                    pool.tensor_tensor(w[:, :, i], codes[:, :, i], s, ALU.mult).then_inc(scaled, 1)

            def root(b, ln):
                pool.wait_ge(var_ready, LN_COUNT[b, ln])
                if (b, ln) == (0, 0):
                    pool.wait_ge(minus_half_made, 1)
                if b >= CB or ln > 0:
                    pool.wait_ge(normed_ready, HALVES * LN_COUNT[(b, 0) if ln else (b - CB, 1)])
                pool.tensor_tensor(rstd[:, b % CB, :], var_eps[:, b % CB, :], minus_half[:, :],
                                   ALU.pow).then_inc(rstd_ready, 1)

            def low_part(s):
                pool.wait_ge(inter_hi, s + 1)
                if s >= 2:
                    pool.wait_ge(down_done, s - 1)
                pool.tensor_tensor(act_lo[:, s % 2, :], act[:, s % RING, :],
                                   act_hi[:, s % RING, :].bitcast(F32), ALU.subtract).then_inc(inter_lo, 1)

            root(0, 0)
            pool.wait_ge(mask_made, 2)
            pool.tensor_tensor(allowed[:, :, :], hits[:, 0], hits[:, 1], ALU.add).then_inc(mask_made, 1)
            root(1, 0)
            scale_unit(0)
            scale_unit(1)
            root(0, 1)
            root(1, 1)
            scale_unit(2)
            for c in range(CHUNKS):
                for n in range(UNITS):
                    if c * UNITS + n >= 1:
                        low_part(c * UNITS + n - 1)
                    if c == 0 and n + DECODE_LEAD < UNITS:
                        scale_unit(n + DECODE_LEAD)
                    for b in next_sequences(c, n, STATS_1):
                        root(b, 0)
                    for b in next_sequences(c, n, STATS_2):
                        root(b, 1)
            low_part(CHUNKS * UNITS - 1)

        @block.scalar
        def _(sc):
            sc.dma_start(router_sb[:, :], router).then_inc(router_loaded, 16)
            sc.dma_start(wq_sb[:, :, :], w_q.rearrange("(k p) d -> p k d", p=P)).then_inc(wq_loaded, 16)
            sc.wait_ge(router_turned, 1)
            sc.activation(router_t[:, :, :], acc_ps[:, 0, 0:KT * SETS].rearrange("p (k n) -> p k n", k=KT),
                          ACT.Copy).then_inc(router_copied, 1)

            def compact(u):
                if u % PG == 0:
                    sc.wait_ge(packed_loaded[u // PG], 16 * 4)
                if u >= 2:
                    sc.wait_ge(unpacked, u - 1)
                sc.activation(code_bytes[:, u % 2, :].bitcast(U8),
                              packed[:, u % PRING, :].bitcast(U8).rearrange("p (j b) -> p j b", b=4)[:, :, 0],
                              ACT.Copy).then_inc(compacted, 1)

            def unit_high(u):
                sc.wait_ge(unit_turned, u + 1)
                for b in range(2):
                    sc.activation(w_hi[:, u, b * WU // 2:(b + 1) * WU // 2], turned_unit(u)[:, b, 0:WU // 2],
                                  ACT.Copy, scale=FP4_SHIFT).then_inc(hi_stored, 1)

            def normalise(b, ln):
                sc.wait_ge(shift_ready, LN_COUNT[b, ln])
                if b >= CB or ln > 0:
                    if ln > 0:
                        sc.wait_ge(ln1_turned, b + 1)
                    else:
                        sc.wait_ge(ln2_turned, b - CB + 1)
                for h in range(HALVES):
                    into, src = normed[:, b % CB, h, :], x_sb[:, b * HALVES + h, :]
                    if ln > 0:
                        into = into.rearrange("p (k i j) -> p k i j", k=KT, i=2)
                        src = src.rearrange("p (k j i) -> p k i j", k=KT, i=2)
                    i = sc.activation(into, src, ACT.Identity,
                                      bias=shift[:, b % CB, h:h + 1], scale=rstd[:, b % CB, h:h + 1])
                    i.then_inc(normed_ready, 1)

            def half(b):
                return misc_ps[:, b % CB, :].rearrange("p (k t) -> p k t", k=KT)

            def ln1_out(b):
                sc.wait_ge(ln1_turned, b + 1)
                sc.activation(ln1_t[:, b % CB, :, :], half(b), ACT.Copy).then_inc(ln1_copied, 1)

            def lead_out(b):
                sc.wait_ge(lead_ready, b + 1)
                sc.activation(lead_tanh[:, b % CB, :], lead[:, b % CB, :], ACT.Tanh, scale=0.5).then_inc(lead_tanh_ready, 1)

            def probs_out(b):
                sc.wait_ge(probs_turned, b + 1)
                sc.activation(probs_t[:, b % CB, :], misc_ps[0:SETS, b % CB, 0:ST], ACT.Copy).then_inc(probs_copied, 1)

            def ln2_high(b):
                sc.wait_ge(ln2_turned, b + 1)
                at = b % CB * ST
                sc.activation(xt_hi[:, b // CB, :, at:at + ST], half(b), ACT.Copy).then_inc(xt_hi_ready, 1)

            def acc_out(c, slices):
                sc.wait_ge(down_done, UNITS * (c + 1))
                if c > 0:
                    sc.wait_ge(out_turned, CB * c)
                for a in slices:
                    sc.activation(out_t[:, a, :], acc_ps[:, a, :], ACT.Copy, scale=gates[:, 1:2]).then_inc(acc_copied, 1)

            def square(s):
                sc.wait_ge(gate_done, s + 1)
                if s >= RING:
                    sc.wait_ge(inter_lo, s - RING + 1)
                sc.activation(act[:, s % RING, :], gate_ps[:, s % 2, :], ACT.Square)
                if s >= 2:
                    sc.wait_ge(inter_done, s - 1)
                sc.activation(half_gu[:, s % 2, :], gate_ps[:, s % 2, :], ACT.Copy, scale=0.5).then_inc(halved, 1)

            def tanh(s):
                sc.wait_ge(cubic_done, s + 1)
                sc.activation(act[:, s % RING, :], act[:, s % RING, :], ACT.Tanh,
                              scale=2.0 * GELU_SCALE * GELU_CUBIC).then_inc(tanh_done, 1)

            def high_part(s):
                sc.wait_ge(inter_done, s + 1)
                if s >= RING:
                    sc.wait_ge(down_done, s - RING + 1)
                sc.activation(act_hi[:, s % RING, :], act[:, s % RING, :], ACT.Copy).then_inc(inter_hi, 1)

            normalise(0, 0)
            normalise(1, 0)
            sc.wait_ge(small_loaded, 16 * 3)
            sc.activation(gates[:, :], gates_in[:, :], ACT.Tanh).then_inc(gates_ready, 1)
            sc.wait_ge(score_w_done, 1)
            sc.activation(score_w[:, :, :], acc_ps[:, 1, 0:KT * SETS].rearrange("p (k n) -> p k n", k=KT),
                          ACT.Copy).then_inc(score_w_copied, 1)
            ln1_out(0)
            compact(0)
            ln1_out(1)
            compact(1)
            for b in range(CB):
                lead_out(b)
            unit_high(0)
            for b in range(CB):
                probs_out(b)
            compact(2)
            unit_high(1)
            for b in range(CB):
                normalise(b, 1)
            for b in range(CB):
                ln2_high(b)
            compact(3)
            for c in range(CHUNKS):
                for n in range(UNITS):
                    s = c * UNITS + n
                    if c == 0 and LEAD <= n + 1 < UNITS:
                        unit_high(n + 1)
                    square(s)
                    for b in next_sequences(c, n, WEIGH):
                        lead_out(b)
                    if c == 0 and n + COMPACT_LEAD < UNITS:
                        compact(n + COMPACT_LEAD)
                    if s >= 1:
                        high_part(s - 1)
                    for b in next_sequences(c, n, CENTER_1):
                        normalise(b, 0)
                    for b in next_sequences(c, n, CENTER_2):
                        normalise(b, 1)
                    for b in next_sequences(c, n, TURN_1):
                        ln1_out(b)
                    for b in next_sequences(c, n, TURN_PROBS):
                        probs_out(b)
                    for b in next_sequences(c, n, TURN_2):
                        ln2_high(b)
                    tanh(s)
                    if c > 0 and n == LAG - 1:
                        acc_out(c - 1, range(KT))
            high_part(CHUNKS * UNITS - 1)
            acc_out(CHUNKS - 1, range(KT - 1))

        @block.vector
        def _(dve):
            reached = {}

            def mark(done, ins):
                reached[done] = len(reached) + 1
                ins.then_inc(attn, 1)

            def after(done):
                dve.wait_ge(attn, reached[done])

            def tile_stats(b, ln):
                if ln > 0:
                    dve.wait_ge(x_updated, b + 1)
                elif b < CB:
                    dve.wait_ge(x_loaded[b], 16)
                elif b == CB:
                    dve.wait_ge(x_rest_loaded, 16)
                for h in range(HALVES):
                    i = dve.bn_stats(stats[:, b % CB, h, :], x_sb[:, b * HALVES + h, :])
                mark(("stats", b, ln), i)

            def aggregate(b, ln):
                after(("stats", b, ln))
                for h in range(HALVES):
                    i = dve.bn_aggr(mean_var[:, b % CB, h, :], stats[:, b % CB, h, :])
                mark(("mean_var", b, ln), i)

            def add_eps(b, ln):
                after(("mean_var", b, ln))
                dve.tensor_scalar(var_eps[:, b % CB, :], mean_var[:, b % CB, :, 1], LN_EPS, None,
                                  ALU.add).then_inc(var_ready, 1)

            def center(b, ln):
                q = b % CB
                dve.wait_ge(rstd_ready, LN_COUNT[b, ln])
                dve.scalar_tensor_tensor(shift[:, q, :], mean_var[:, q, :, 0], -1.0, rstd[:, q, :],
                                         ALU.mult, ALU.mult).then_inc(shift_ready, 1)

            def read_scores(b):
                q = b % CB
                dve.wait_ge(scores_done, b + 1)
                dve.scalar_tensor_tensor(
                    scores[:, q, :, :].rearrange("p h n -> p (h n)"), misc_ps[:, q, 0:HALVES * SETS], SCORE_SCALE,
                    score_bias[:, :, :].rearrange("p h n -> p (h n)"), ALU.mult, ALU.add).then_inc(scores_read, 1)

            def find_top(b):
                dve.wait_ge(scores_read, b + 1)
                for h in range(HALVES):
                    i = dve.max(top8[:, b % CB, h, :], scores[:, b % CB, h, :])
                mark(("top8", b), i)

            def find_lead(b):
                q = b % CB
                after(("top8", b))
                dve.tensor_tensor(lead[:, q, :], top8[:, q, :, 0], top8[:, q, :, 1], ALU.subtract).then_inc(lead_ready, 1)

            def find_where(b):
                q = b % CB
                after(("top8", b))
                for h in range(HALVES):
                    i = dve.max_index(top8_at[:, q, h, :], top8[:, q, h, :], scores[:, q, h, :])
                mark(("top8_at", b), i)

            def top_two(b):
                q = b % CB
                after(("top8_at", b))
                dve.tensor_copy(top2_at[:, q, :, :], top8_at[:, q, :, 0:2])

            def weigh(b):
                q = b % CB
                dve.wait_ge(lead_tanh_ready, b + 1)
                dve.tensor_scalar(w_first[:, q, :], lead_tanh[:, q, :], 1.0, half_gate[:, 0:1], ALU.add, ALU.mult)
                mark(("weights", b), dve.tensor_scalar(w_second[:, q, :], lead_tanh[:, q, :], half_gate[:, 1:2],
                                                       half_gate[:, 0:1], ALU.mult, ALU.add))

            def spread(b):
                q = b % CB
                after(("weights", b))
                for h in range(HALVES):
                    dve.tensor_scalar(probs_a[:, h, :], iota_f[:, :], top2_at[:, q, h, 0:1], w_first[:, q, h:h + 1],
                                      ALU.is_equal, ALU.mult)
                    i = dve.tensor_scalar(probs_b[:, h, :], iota_f[:, :], top2_at[:, q, h, 1:2],
                                          w_second[:, q, h:h + 1], ALU.is_equal, ALU.mult)
                mark(("spread", b), i)

            def join(b):
                after(("spread", b))
                dve.tensor_tensor(probs[:, b % CB, :, :], probs_a[:, :, :], probs_b[:, :, :],
                                  ALU.add).then_inc(probs_ready, 1)

            def tiles(b):
                return x_sb[:, b * HALVES:(b + 1) * HALVES, :].rearrange("p t d -> p (t d)")

            def add_attention(b):
                dve.wait_ge(attended, b + 1)
                dve.tensor_tensor(tiles(b), misc_ps[:, b % CB, :], tiles(b), ALU.add).then_inc(x_updated, 1)

            def ln2_low(b):
                dve.wait_ge(xt_hi_ready, b + 1)
                at = b % CB * ST
                dve.tensor_tensor(xt_lo[:, b // CB, :, at:at + ST],
                                  misc_ps[:, b % CB, :].rearrange("p (k t) -> p k t", k=KT),
                                  xt_hi[:, b // CB, :, at:at + ST].bitcast(F32), ALU.subtract).then_inc(xt_lo_ready, 1)

            def add_output(b):
                dve.wait_ge(out_turned, b + 1)
                dve.tensor_tensor(tiles(b), misc_ps[:, b % CB, :], tiles(b), ALU.add).then_inc(out_ready, 1)

            def unpack(u, stage):
                both = nibbles[:, :, :, :].rearrange("p g i j -> p (g i j)")
                words = code_bytes[:, u % 2, :].rearrange("p (g j) -> p g j", g=WU // P)
                if stage == 0:
                    dve.wait_ge(compacted, u + 1)
                    if u > 0:
                        dve.wait_ge(unpacked, u)
                    dve.tensor_scalar(nibbles[:, :, 0, :], words, LOW_NIBBLES, None, ALU.bitwise_and)
                    dve.tensor_scalar(nibbles[:, :, 1, :], words, 4, LOW_NIBBLES,
                                      ALU.logical_shift_right, ALU.bitwise_and).then_inc(lined_up, 1)
                elif stage == 1:
                    dve.wait_ge(lined_up, 2 * u + 1)
                    dve.scalar_tensor_tensor(both, both, 3, both, ALU.logical_shift_left,
                                             ALU.bitwise_or).then_inc(lined_up, 1)
                else:
                    dve.wait_ge(lined_up, 2 * u + 2)
                    if u >= 2:
                        dve.wait_ge(scaled, 2 * (u - 1))
                    dve.tensor_scalar(code_bits[:, u % 2, :], both, 1, CODE_BITS,
                                      ALU.logical_shift_left, ALU.bitwise_and).then_inc(unpacked, 1)

            def unit_low(u):
                dve.wait_ge(hi_stored, 2 * (u + 1))
                for b in range(2):
                    part = slice(b * WU // 2, (b + 1) * WU // 2)
                    dve.scalar_tensor_tensor(w_lo[:, u, part], turned_unit(u)[:, b, 0:WU // 2], FP4_SHIFT,
                                             w_hi[:, u, part].bitcast(F32), ALU.mult,
                                             ALU.subtract).then_inc(lo_stored, 1)

            def cubic(s):
                dve.wait_ge(halved, s + 1)
                a = act[:, s % RING, :]
                dve.scalar_tensor_tensor(a, a, 1.0 / GELU_CUBIC, half_gu[:, s % 2, :], ALU.add,
                                         ALU.mult).then_inc(cubic_done, 1)

            def gate_up(s):
                dve.wait_ge(up_done, s + 1)
                dve.wait_ge(cubic_done, s + 1)
                h = half_gu[:, s % 2, :]
                dve.tensor_tensor(h, up_ps[:, s % 2, :], h, ALU.mult).then_inc(gated_up, 1)

            def combine(s):
                dve.wait_ge(tanh_done, s + 1)
                dve.wait_ge(gated_up, s + 1)
                a = act[:, s % RING, :]
                dve.scalar_tensor_tensor(a, a, 1.0, half_gu[:, s % 2, :], ALU.add, ALU.mult).then_inc(inter_done, 1)

            tile_stats(0, 0)
            dve.wait_ge(iota_made, 1)
            dve.wait_ge(tokens_loaded, 16)
            dve.tensor_tensor(hits, tok_sb[:, :, :].rearrange("p h k -> p k h").unsqueeze(3)
                              .to_broadcast([P, PICKS, HALVES, SETS]),
                              iota_i[:, :].unsqueeze(1).unsqueeze(1).to_broadcast([P, PICKS, HALVES, SETS]),
                              ALU.is_equal).then_inc(mask_made, 1)
            aggregate(0, 0)
            tile_stats(1, 0)
            add_eps(0, 0)
            aggregate(1, 0)
            dve.tensor_copy(iota_f[:, :], iota_i[:, :])
            add_eps(1, 0)
            center(0, 0)
            dve.wait_ge(small_loaded, 16 * 3)
            dve.tensor_copy(bq_wide[:, :, :], bq_sb[:, :].unsqueeze(2).to_broadcast([P, KT, P])).then_inc(bq_spread, 1)
            center(1, 0)
            dve.wait_ge(mask_made, 3)
            dve.tensor_scalar(allowed[:, :, :], allowed[:, :, :], 0.5, MASKED, ALU.is_lt, ALU.mult).then_inc(mask_made, 1)
            dve.wait_ge(mask_made, 4)
            dve.wait_ge(score_w_copied, 1)
            cb = acc_ps[:, 1, KT * SETS:(KT + 1) * SETS].unsqueeze(1).to_broadcast([P, HALVES, SETS])
            mark("score_bias", dve.scalar_tensor_tensor(score_bias[:, :, :], cb, SCORE_SCALE, allowed[:, :, :],
                                                        ALU.mult, ALU.add))
            for stage in range(3):
                unpack(0, stage)
            after("score_bias")
            dve.wait_ge(gates_ready, 1)
            for i, sign in enumerate((0.5, -0.5)):
                dve.tensor_scalar(half_gate[:, i:i + 1], gates[:, 0:1], sign, None, ALU.mult)
            read_scores(0)
            find_top(0)
            find_lead(0)
            find_where(0)
            read_scores(1)
            top_two(0)
            find_top(1)
            weigh(0)
            find_lead(1)
            spread(0)
            find_where(1)
            join(0)
            top_two(1)
            weigh(1)
            spread(1)
            join(1)
            for stage in range(3):
                unpack(1, stage)
            unit_low(0)
            add_attention(0)
            unpack(2, 0)
            tile_stats(0, 1)
            unpack(2, 1)
            aggregate(0, 1)
            add_attention(1)
            add_eps(0, 1)
            tile_stats(1, 1)
            center(0, 1)
            aggregate(1, 1)
            unpack(2, 2)
            add_eps(1, 1)
            unit_low(1)
            center(1, 1)
            ln2_low(0)
            ln2_low(1)

            for c in range(CHUNKS):
                for n in range(UNITS):
                    s = c * UNITS + n
                    ahead = n + DECODE_LEAD if c == 0 and n + DECODE_LEAD < UNITS else None

                    def attention(*parts):
                        for stage, part, *ln in parts:
                            for b in next_sequences(c, n, stage):
                                part(b, *ln)

                    if c == 0 and LEAD <= n + 1 < UNITS:
                        unit_low(n + 1)
                    attention((CENTER_1, center, 0), (CENTER_2, center, 1), (STATS_1, tile_stats, 0),
                              (STATS_2, tile_stats, 1), (WEIGH, find_where), (SPREAD, spread))
                    if ahead:
                        unpack(ahead, 0)
                    cubic(s)
                    attention((STATS_1, aggregate, 0), (STATS_2, aggregate, 1), (WEIGH, top_two), (SPREAD, join))
                    if ahead:
                        unpack(ahead, 1)
                    gate_up(s)
                    attention((STATS_1, add_eps, 0), (STATS_2, add_eps, 1), (WEIGH, weigh), (SCORE, read_scores),
                              (ATTEND, add_attention), (TURN_2, ln2_low))
                    if ahead:
                        unpack(ahead, 2)
                    attention((SCORE, find_top),)
                    combine(s)
                    attention((SCORE, find_lead),)
                    if c > 0 and n in AT_OUT:
                        add_output((c - 1) * CB + AT_OUT.index(n))
            dve.wait_ge(down_done, UNITS * CHUNKS)
            dve.wait_ge(out_turned, CB * (CHUNKS - 1))
            dve.tensor_scalar(out_t[:, KT - 1, :], acc_ps[:, KT - 1, :], gates[:, 1:2], None,
                              ALU.mult).then_inc(acc_copied, 1)
            for b in range((CHUNKS - 1) * CB, BATCH):
                add_output(b)

        @block.tensor
        def _(pe):
            def turn_router():
                pe.wait_ge(ident_made, 2)
                pe.wait_ge(router_loaded, 16)
                for k in range(KT):
                    i = pe.transpose(acc_ps[:, 0, k * SETS:(k + 1) * SETS], router_sb[:, k * P:(k + 1) * P],
                                     ident[0:SETS, 0:SETS])
                i.then_inc(router_turned, 1)

            def fold_router():
                pe.wait_ge(router_copied, 1)
                pe.wait_ge(wq_loaded, 16)
                for k in range(KT):
                    for e in range(KT):
                        pe.matmul(acc_ps[:, 1, k * SETS:(k + 1) * SETS], wq_sb[:, e, k * P:(k + 1) * P],
                                  router_t[:, e, :], start=(e == 0), stop=(e == KT - 1))
                pe.wait_ge(bq_spread, 1)
                for e in range(KT):
                    i = pe.matmul(acc_ps[:, 1, KT * SETS:(KT + 1) * SETS], bq_wide[:, e, :], router_t[:, e, :],
                                  start=(e == 0), stop=(e == KT - 1))
                i.then_inc(score_w_done, 1)

            def turn_normed(b, ln, done):
                for h in range(HALVES):
                    pe.wait_ge(normed_ready, HALVES * (LN_COUNT[b, ln] - 1) + h + 1)
                    for k in range(KT):
                        at = k * ST + h * P
                        i = pe.transpose(misc_ps[:, b % CB, at:at + P], normed[:, b % CB, h, k * P:(k + 1) * P], ident[:, :])
                i.then_inc(done, 1)

            def score(b):
                pe.wait_ge(ln1_copied, b + 1)
                if b == 0:
                    pe.wait_ge(score_w_copied, 1)
                for h in range(HALVES):
                    for k in range(KT):
                        i = pe.matmul(misc_ps[:, b % CB, h * SETS:(h + 1) * SETS], ln1_t[:, b % CB, k, h * P:(h + 1) * P],
                                      score_w[:, k, :], start=(k == 0), stop=(k == KT - 1))
                i.then_inc(scores_done, 1)

            def turn_probs(b):
                pe.wait_ge(probs_ready, b + 1)
                for h in range(HALVES):
                    i = pe.transpose(misc_ps[0:SETS, b % CB, h * P:(h + 1) * P], probs[:, b % CB, h, :], ident[:, :])
                i.then_inc(probs_turned, 1)

            def attend(b):
                pe.wait_ge(probs_copied, b + 1)
                if b == 0:
                    pe.wait_ge(ctx_loaded, 16)
                if b == CB:
                    pe.wait_ge(ctx_rest_loaded, 16)
                for h in range(HALVES):
                    i = pe.matmul(misc_ps[:, b % CB, h * D:(h + 1) * D], probs_t[:, b % CB, h * P:(h + 1) * P],
                                  ctx_sb[:, b, :], start=True, stop=True)
                i.then_inc(attended, 1)

            def turn_unit(u):
                pe.wait_ge(scaled, 2 * (u + 1))
                for i6 in range(WU // P):
                    b, at = divmod(i6 * P, WU // 2)
                    into = turned_unit(u)[:, b, at:at + P]
                    if i6 < 2 * KT:
                        into = into.rearrange("p (i j) -> p j i", i=2)
                    i = pe.transpose(into, w_nat[:, u % 2, i6 * P:(i6 + 1) * P], ident[:, :])
                i.then_inc(unit_turned, 1)

            def unit_copied(u):
                pe.wait_ge(hi_stored, 2 * (u + 1))
                pe.wait_ge(lo_stored, 2 * (u + 1))

            def project(c, n, m, into, tok=slice(0, TOK)):
                first, last = True, (KT - 1, 2)
                for k in range(KT):
                    w = slice(m * D + k * P, m * D + (k + 1) * P)
                    for j, (wt, xt) in enumerate(((w_hi, xt_hi), (w_hi, xt_lo), (w_lo, xt_hi))):
                        i = pe.matmul(into[:, tok], wt[:, n, w], xt[:, c, k, tok], start=first, stop=(k, j) == last)
                        first = False
                return i

            def down(s):
                c, n = divmod(s, UNITS)
                pe.wait_ge(inter_hi, s + 1)
                if n == 0 and c > 0:
                    pe.wait_ge(acc_copied, KT * c)
                for part in range(3):
                    if part == 2:
                        pe.wait_ge(inter_lo, s + 1)
                    for a in range(KT):
                        wt = w_lo if part == 1 else w_hi
                        h = act_lo[:, s % 2, :] if part == 2 else act_hi[:, s % RING, :]
                        i = pe.matmul(acc_ps[:, a, :], wt[:, n, 2 * D + a * P:2 * D + (a + 1) * P], h,
                                      start=(n == 0 and part == 0), stop=(n == UNITS - 1 and part == 2))
                i.then_inc(down_done, 1)

            def turn_output(b):
                pe.wait_ge(acc_copied, KT * (b // CB + 1))
                if b >= CB:
                    pe.wait_ge(out_ready, b - CB + 1)
                for h in range(HALVES):
                    for a in range(KT):
                        at = h * D + a * P
                        t = (b % CB * HALVES + h) * P
                        i = pe.transpose(misc_ps[:, b % CB, at:at + P], out_t[:, a, t:t + P], ident[:, :])
                i.then_inc(out_turned, 1)

            turn_router()
            fold_router()
            for b in range(CB):
                turn_normed(b, 0, ln1_turned)
            for b in range(CB):
                score(b)
            turn_unit(0)
            for b in range(CB):
                turn_probs(b)
            for b in range(CB):
                attend(b)
            turn_unit(1)
            for b in range(CB):
                turn_normed(b, 1, ln2_turned)

            for c in range(CHUNKS):
                for n in range(UNITS):
                    s = c * UNITS + n
                    if c == 0:
                        unit_copied(max(n, 1))
                    if s == 0:
                        for b in range(CB):
                            pe.wait_ge(xt_lo_ready, b + 1)
                            tok = slice(b * ST, (b + 1) * ST)
                            gate = project(c, n, 0, gate_ps[:, 0, :], tok)
                            up = project(c, n, 1, up_ps[:, 0, :], tok)
                        gate.then_inc(gate_done, 1)
                        up.then_inc(up_done, 1)
                    else:
                        if n == 0:
                            pe.wait_ge(xt_lo_ready, CB * (c + 1))
                        if s >= 2:
                            pe.wait_ge(halved, s - 1)
                        project(c, n, 0, gate_ps[:, n % 2, :]).then_inc(gate_done, 1)
                        if s >= 2:
                            pe.wait_ge(gated_up, s - 1)
                        project(c, n, 1, up_ps[:, n % 2, :]).then_inc(up_done, 1)

                    left = None
                    for stage, run, done in (
                        (TURN_1, lambda b: turn_normed(b, 0, ln1_turned), ln1_copied),
                        (SCORE, score, scores_read),
                        (TURN_PROBS, turn_probs, probs_copied),
                        (ATTEND, attend, x_updated),
                        (TURN_2, lambda b: turn_normed(b, 1, ln2_turned), xt_lo_ready),
                    ):
                        for b in next_sequences(c, n, stage):
                            if c == 0:
                                unit_copied(min(n + LEAD - 1, UNITS - 1))
                            elif stage == TURN_1:
                                pe.wait_ge(out_ready, CB * (c - 1))
                            run(b)
                            left = (done, b + 1)
                    if c > 0 and n in AT_OUT:
                        b = (c - 1) * CB + AT_OUT.index(n)
                        if c + 1 < CHUNKS:
                            pe.wait_ge(xt_lo_ready, b + 2 * CB + 1)
                        turn_output(b)

                    if s >= LAG:
                        down(s - LAG)

                    if c == 0 and n + LEAD < UNITS:
                        unit_copied(n + LEAD - 1)
                        if left:
                            pe.wait_ge(*left)
                        turn_unit(n + LEAD)
            for s in range(CHUNKS * UNITS - LAG, CHUNKS * UNITS):
                down(s)
            for b in range((CHUNKS - 1) * CB, BATCH):
                turn_output(b)


_INS = ["x", "ctx_2048", "itok_Sx4_0_63", "g_xattn", "g_ffn", "L0_xattn_desc_router", "L0_xattn_W_q", "L0_xattn_b_q",
        "L0_ffn_gate_W_packed", "L0_ffn_gate_scales", "L0_ffn_up_W_packed", "L0_ffn_up_scales",
        "L0_ffn_down_W_packed", "L0_ffn_down_scales"]
_OUTS = [((8, 256, 256), "float32")]


def kernel(**inputs):
    import numpy as _np
    import concourse.bacc as _bacc
    from concourse import mybir as _mybir
    from concourse.bass_utils import run_bass_kernel_spmd as _run

    nc = _bacc.Bacc("TRN2", target_bir_lowering=False, num_devices=1)
    arrays, args = {}, []
    for name in _INS:
        a = _np.ascontiguousarray(inputs[name])
        arrays[f"in_{name}_dram"] = a
        args.append(nc.dram_tensor(f"in_{name}_dram", a.shape, _mybir.dt.from_np(a.dtype), kind="ExternalInput").ap())
    for i, (shape, dtype) in enumerate(_OUTS):
        dt = _mybir.dt.from_np(_np.dtype(dtype))
        args.append(nc.dram_tensor(f"out_{i}_dram", shape, dt, kind="ExternalOutput").ap())
    build_program(nc, *args)
    r = _run(nc, [arrays], core_ids=[0])
    got = tuple(r.results[0][f"out_{i}_dram"] for i in range(len(_OUTS)))
    return got[0]
```
